# Optimizing a Trainium2 kernel written in Bass

```python
import numpy as np
import jax
import jax.numpy as jnp

def _softmax(x, axis=-1):
    return jax.nn.softmax(x, axis=axis)

def _gelu(x):
    return jax.nn.gelu(x, approximate=True)

def _silu(x):
    return jax.nn.silu(x)

def _sigmoid(x):
    return jax.nn.sigmoid(x)

def _layernorm(x, axis=-1, eps=1e-05):
    m = jnp.mean(x, axis=axis, keepdims=True)
    v = jnp.var(x, axis=axis, keepdims=True)
    return (x - m) / jnp.sqrt(v + eps)

def _scatter_add(tgt, idx, src, axis=0):
    return tgt.at[idx].add(src)

def _segment_sum(src, seg, n):
    return jax.ops.segment_sum(src, seg, n)
kernel_name = 'mk_adj_preln_d1_adj_r2_38cd06'

def setup_inputs(seed: int=0):
    np.random.seed(seed)
    _w = jnp.asarray

    def _rec_inputs():
        import jax
        import jax.numpy as jnp
        _gk = jax.random.key(seed)
        x = 7.22e-05 + 1 * jax.random.normal(jax.random.fold_in(_gk, 1), (128, 128, 512), jnp.float32)
        _a = jax.random.bernoulli(jax.random.fold_in(_gk, 2), 0.03125, (128, 128, 128))
        _a = jnp.logical_or(_a, jnp.swapaxes(_a, -1, -2))
        _a = jnp.logical_or(_a, jnp.eye(128, dtype=bool))
        _af = _a.astype(jnp.float32)
        _af = _af * jax.random.uniform(jax.random.fold_in(_gk, 3), (128, 128, 128), jnp.float32, 0.05, 4.42607)
        adj = _af
        return (x, adj)
    x, adj = _rec_inputs()

    def _L0_gnn_setup():
        import jax, jax.numpy as jnp
        import numpy as np
        NUM_HEADS = 16
        key = jax.random.key(seed)
        ks = jax.random.split(key, 7)
        B, N, D = (16, 256, 512)
        return {'x': jax.random.normal(ks[0], (B, N, D), dtype=jnp.float32), 'spatial_encoding': jax.random.normal(ks[1], (B, N, N), dtype=jnp.float32), 'edge_encoding': jax.random.normal(ks[2], (B, N, N), dtype=jnp.float32), 'Wq': jax.random.normal(ks[3], (D, D), dtype=jnp.float32) * D ** (-0.5), 'Wk': jax.random.normal(ks[4], (D, D), dtype=jnp.float32) * D ** (-0.5), 'Wv': jax.random.normal(ks[5], (D, D), dtype=jnp.float32) * D ** (-0.5), 'Wo': jax.random.normal(ks[6], (D, D), dtype=jnp.float32) * D ** (-0.5)}
    _L0_gnn_all = _L0_gnn_setup()
    _L0_gnn_in = {k: v for k, v in _L0_gnn_all.items() if k in ('Wq', 'Wk', 'Wv', 'Wo')}
    del _L0_gnn_all
    return {'x': x, 'adj': adj, 'L0_gnn_Wq': _L0_gnn_in['Wq'], 'L0_gnn_Wk': _L0_gnn_in['Wk'], 'L0_gnn_Wv': _L0_gnn_in['Wv'], 'L0_gnn_Wo': _L0_gnn_in['Wo']}

def reference(x, adj, L0_gnn_Wq, L0_gnn_Wk, L0_gnn_Wv, L0_gnn_Wo):
    import jax
    import jax.numpy as jnp

    def _L0_gnn_ref(x, spatial_encoding, edge_encoding, Wq, Wk, Wv, Wo):
        import jax, jax.numpy as jnp
        import numpy as np
        NUM_HEADS = 16
        B, N, D = x.shape
        H = NUM_HEADS
        hd = D // H
        scale = D ** (-0.5)

        def split_heads(t):
            return t.reshape(B, N, H, hd).transpose(0, 2, 1, 3)
        q = split_heads(x @ Wq.T)
        k = split_heads(x @ Wk.T)
        v = split_heads(x @ Wv.T)
        bias = (spatial_encoding + edge_encoding)[:, None]
        a = jnp.einsum('bhnd,bhmd->bhnm', q, k) * scale + bias
        row_nonzero = jnp.any(a != 0, axis=-1, keepdims=True)
        a = jnp.where(row_nonzero, a, -jnp.inf)
        p = jax.nn.softmax(a, axis=-1)
        p = jnp.where(jnp.isnan(p), 0.0, p)
        o = jnp.einsum('bhnm,bhmd->bhnd', p, v)
        o = o.transpose(0, 2, 1, 3).reshape(B, N, D)
        return o @ Wo.T
    h = jnp.maximum(_layernorm(x, axis=-1), 0.0)
    x = x + _L0_gnn_ref(h, adj, adj, L0_gnn_Wq, L0_gnn_Wk, L0_gnn_Wv, L0_gnn_Wo)
    return x

_drawn_inputs = setup_inputs


def setup_inputs(seed=0):
    import zlib

    import numpy as np

    out = dict(_drawn_inputs(seed))
    spreads = {}
    factors = {'L0_gnn_Wq': 2.917, 'L0_gnn_Wk': 2.876}
    for name, (base, spread) in spreads.items():
        noise = np.random.default_rng([zlib.crc32(name.encode()), seed]).standard_normal(out[name].shape)
        drawn = base * np.exp(spread * noise) if base else spread * noise
        out[name] = jnp.asarray(drawn.astype(out[name].dtype))
    for name, factor in factors.items():
        out[name] = (out[name] * factor).astype(out[name].dtype)
    return out
```

```python
from contextlib import ExitStack

import concourse.bass as bass
from concourse import mybir

ALU = mybir.AluOpType
ACT = mybir.ActivationFunctionType
AX = mybir.AxisListType
F32 = mybir.dt.float32
F32R = mybir.dt.float32r

P = 128
HEADS = 16
BODY = 4
LEAD = 5
EPS = 1e-5


class Batch:

    def __init__(self, group, place):
        self.group = group + place // BODY
        self.place = place % BODY

    def __add__(self, k):
        return Batch(self.group, self.place + k)

    def __sub__(self, k):
        return Batch(self.group, self.place - k)

    def count(self, per_batch, more=0):
        return self.group * (BODY * per_batch) + (self.place * per_batch + more)

    def within(self, n):
        return not isinstance(self.group, int) or 0 <= BODY * self.group + self.place < n

    @property
    def parity(self):
        return self.place % 2

    @property
    def pair_parity(self):
        return self.place // 2

    @property
    def of_pair(self):
        return Batch(self.group, self.place - self.place % 2)


def preln_graph_attention(nc, x, adj, wqT, wkT, wvT, woT, out):
    B, N, D = x.shape
    assert N == P and D % P == 0 and B % BODY == 0
    HD = D // HEADS
    KC = D // P
    R = P // HD
    assert HEADS == R * KC
    SCALE = float(D) ** -0.5
    PAIR = 2 * N
    FIRST, LAST = 1, B // BODY - 2

    ctx = ExitStack()

    def sb(name, shape, dt=F32):
        return ctx.enter_context(nc.sbuf_tensor(name, shape, dt))

    def sem(name):
        return ctx.enter_context(nc.semaphore(name))

    x_of = x.rearrange("(g s) n d -> g s n d", s=BODY)
    adj_of = adj.rearrange("(g s) n m -> g s n m", s=BODY)
    out_of = out.rearrange("(g s) n d -> g s n d", s=BODY)

    with ctx:
        W_NAMES = ("q", "k", "v", "o")
        w_hi = [sb(f"w_hi_{n}", [P, KC, D], F32R) for n in W_NAMES]
        w_lo = [sb(f"w_lo_{n}", [P, KC, D], F32R) for n in W_NAMES]
        xs = sb("xs", [P, 2, BODY, D])
        adjs = sb("adjs", [P, BODY, N])
        adj2 = sb("adj2", [P, 2, N])
        stats = sb("stats", [P, 2, 6])
        moments = sb("moments", [P, 2, 2])
        rstd = sb("rstd", [P, 2, 2])
        hn = sb("hn", [P, 2, D])
        h_hi = [sb(f"h_hi{i}", [P, KC, PAIR], F32R) for i in range(2)]
        h_lo = [sb(f"h_lo{i}", [P, KC, PAIR], F32R) for i in range(2)]
        qk = sb("qk", [P, 2, KC, 2, PAIR])
        vs = sb("vs", [P, BODY, D])
        a = sb("a", [P, 2, HEADS, N])
        pr = sb("pr", [P, 2, HEADS, N])
        negmax = sb("negmax", [P, 2, HEADS])
        absmax = sb("absmax", [P, 2, HEADS])
        sums = sb("sums", [P, 2, HEADS])
        inv = sb("inv", [P, HEADS])
        inv_live = sb("inv_live", [P, 2, HEADS])
        prT = sb("prT", [P, R, KC, N])
        o_hi = sb("o_hi", [P, KC, N], F32R)
        o_lo = sb("o_lo", [P, KC, N], F32R)
        y = sb("y", [P, 2, D])
        ident = sb("ident", [P, P])
        consts = sb("consts", [P, 2])
        stage = [pr[:, 0].rearrange("p h n -> p (h n)"), pr[:, 1].rearrange("p h n -> p (h n)"),
                 a[:, 1].rearrange("p h n -> p (h n)"), prT[:].rearrange("p r c n -> p (r c n)")]

        quad = [ctx.enter_context(nc.psum_tensor(f"quad{r}", [P, KC, N], F32)) for r in range(R)]
        bank_a = ctx.enter_context(nc.psum_tensor("bank_a", [P, D], F32))
        bank_b = ctx.enter_context(nc.psum_tensor("bank_b", [P, D], F32))
        bank_o = ctx.enter_context(nc.psum_tensor("bank_o", [P, KC, N], F32))
        bank_t = ctx.enter_context(nc.psum_tensor("bank_t", [P, KC, N], F32))

        w_in = [sem(f"w_in{i}") for i in range(4)]
        w_high = sem("w_high")
        w_low = sem("w_low")
        x_in = [sem(f"x_in{i}") for i in range(BODY)]
        adj_in = [sem(f"adj_in{i}") for i in range(BODY)]
        out_done = [sem(f"out_done{i}") for i in range(2)]
        ident_set = sem("ident_set")
        const_set = sem("const_set")
        scores_ready = sem("scores_ready")
        qk_ready = sem("qk_ready")
        v_ready = sem("v_ready")
        prT_ready = sem("prT_ready")
        oT_ready = sem("oT_ready")
        rows_ready = sem("rows_ready")
        hT_ready = sem("hT_ready")
        qk_saved = sem("qk_saved")
        v_saved = sem("v_saved")
        prT_saved_act = sem("prT_saved_act")
        oT_high = sem("oT_high")
        hT_high = sem("hT_high")
        exps = sem("exps")
        stats_done = sem("stats_done")
        moments_done = sem("moments_done")
        h_normed = sem("h_normed")
        biased = sem("biased")
        max_done = sem("max_done")
        abs_done = sem("abs_done")
        inv_done = sem("inv_done")
        inv_live_done = sem("inv_live_done")
        prT_saved_dve = sem("prT_saved_dve")
        oT_low = sem("oT_low")
        hT_low = sem("hT_low")
        y_done = sem("y_done")
        adj_doubled = sem("adj_doubled")
        var_eps = sem("var_eps")
        rstd_done = sem("rstd_done")
        normed = sem("normed")

        block = ctx.enter_context(nc.Block())

        def steps(eng, step, weight=None):
            for n in range(-LEAD, BODY * FIRST):
                if weight and n == 2 - LEAD:
                    weight(0)
                    weight(1)
                    weight(2)
                if weight and n == -1:
                    weight(3)
                step(Batch(0, n))
            with eng.Fori(FIRST, LAST, 1) as g:
                for s in range(BODY):
                    step(Batch(g, s))
            for n in range(BODY * LAST, B):
                step(Batch(0, n))

        @block.sync
        def _(sp):
            def load_weight(i, src):
                sp.dma_start(stage[i].rearrange("p (c n) -> p c n", c=KC),
                             src.rearrange("(c p) n -> p c n", p=P)).then_inc(w_in[i], 16)

            def load_x(b, ring_half):
                sp.dma_start(xs[:, ring_half, b.place, :], x_of[b.group, b.place]).then_inc(x_in[b.place], 16)

            def load_adj(b):
                sp.dma_start(adjs[:, b.place, :], adj_of[b.group, b.place]).then_inc(adj_in[b.place], 16)

            load_x(Batch(0, 0), 0)
            load_x(Batch(0, 1), 0)
            load_weight(0, wqT)
            load_weight(1, wkT)
            load_x(Batch(0, 2), 0)
            load_x(Batch(0, 3), 0)
            load_weight(2, wvT)
            for n in range(BODY):
                load_adj(Batch(0, n))
            load_weight(3, woT)
            for n in range(BODY, 2 * BODY):
                sp.wait_ge(stats_done, n - BODY + 1)
                load_x(Batch(0, n), 1)
            for n in range(BODY, BODY + 2):
                sp.wait_ge(adj_doubled, n - BODY + 1)
                load_adj(Batch(0, n))

            def step(t, g, here):
                sp.wait_ge(y_done, t.count(1, 1))
                sp.dma_start(out_of[t.group, t.place], y[:, t.parity, :]).then_inc(out_done[t.parity], 16)
                b = t + 2 * BODY
                if b.within(B):
                    load_x(b, here)
                b = t + (BODY + 2)
                if b.within(B):
                    sp.wait_ge(adj_doubled, (b - BODY).count(1, 1))
                    load_adj(b)

            for n in range(BODY * FIRST):
                step(Batch(0, n), None, (n // BODY) % 2)
            with sp.Fori(FIRST, LAST, 1) as g:
                half = sp.snap(g % 2)
                for s in range(BODY):
                    step(Batch(g, s), g, half)
            for n in range(BODY * LAST, B):
                step(Batch(0, n), None, (n // BODY) % 2)
            sp.wait_ge(out_done[0], 16 * (B // 2))
            sp.wait_ge(out_done[1], 16 * (B // 2))

        @block.tensor
        def _(pe):
            def product3(dst, hi_l, lo_l, hi_r, lo_r, chunks=range(KC)):
                for k in chunks:
                    pe.matmul(dst, hi_l(k), hi_r(k), start=(k == 0), stop=False)
                    pe.matmul(dst, hi_l(k), lo_r(k), start=False, stop=False)
                    last = pe.matmul(dst, lo_l(k), hi_r(k), start=False, stop=(k == KC - 1))
                return last

            def scores(b, chunks):
                if 0 in chunks:
                    pe.wait_ge(qk_saved, b.of_pair.count(2, 4))
                if 0 in chunks and (b - 2).within(B):
                    pe.wait_ge(prT_saved_act, (b - 2).count(2, 2))
                    pe.wait_ge(prT_saved_dve, (b - 2).count(2, 2))
                tok = slice(b.parity * N, b.parity * N + N)
                for c in chunks:
                    for r in range(R):
                        rows = slice(HD * r, HD * r + HD)
                        last = pe.matmul(quad[r][:, c, :], qk[rows, b.pair_parity, c, 0, tok],
                                         qk[rows, b.pair_parity, c, 1, tok], start=True, stop=True)
                if KC - 1 in chunks:
                    last.then_inc(scores_ready, 1)

            def qk_chunk(b, half, bank):
                c = 2 * b.parity + half
                hi, lo = h_hi[b.pair_parity], h_lo[b.pair_parity]
                cols = slice(P * c, P * c + P)
                for i in range(2):
                    last = product3(bank[:, i * PAIR:(i + 1) * PAIR],
                                    lambda k: w_hi[i][:, k, cols], lambda k: w_lo[i][:, k, cols],
                                    lambda k: hi[:, k, :], lambda k: lo[:, k, :])
                last.then_inc(qk_ready, 1)

            def value_rows(b, chunks):
                hi, lo = h_hi[b.pair_parity], h_lo[b.pair_parity]
                tok = slice(b.parity * N, b.parity * N + N)
                last = product3(bank_a[:], lambda k: hi[:, k, tok], lambda k: lo[:, k, tok],
                                lambda k: w_hi[2][:, k, :], lambda k: w_lo[2][:, k, :], chunks)
                if KC - 1 in chunks:
                    last.then_inc(v_ready, 1)

            def step(t):
                b = t + 1
                if b.within(B):
                    scores(b, range(KC // 2))
                b = t + 3
                if b.within(B):
                    pe.wait_ge(hT_low, b.of_pair.count(1, 2))
                    if not (b - 1).within(B):
                        pe.wait_ge(w_high, 2)
                        pe.wait_ge(w_low, 2)
                    if (b - 1).within(B):
                        pe.wait_ge(v_saved, b.count(1))
                    qk_chunk(b, 0, bank_a)
                b = t + 1
                if b.within(B):
                    scores(b, range(KC // 2, KC))
                b = t + 3
                if b.within(B):
                    if (t - 1).within(B):
                        pe.wait_ge(y_done, t.count(1))
                    elif (b - 1).within(B):
                        pe.wait_ge(qk_saved, b.count(2))
                    qk_chunk(b, 1, bank_b)
                if t.within(B):
                    for r in range(R):
                        pe.wait_ge(biased, (t + 1).count(4, r + 1) if (t + 1).within(B) else t.count(4, 4))
                        pe.wait_ge(normed, t.count(4, r + 1))
                        for c in range(KC):
                            last = pe.transpose(quad[r][:, c, :], pr[:, t.parity, KC * r + c, :], ident[:])
                        last.then_inc(prT_ready, 1)
                b = t + 3
                if b.within(B):
                    if not (b - 1).within(B):
                        pe.wait_ge(w_high, 3)
                        pe.wait_ge(w_low, 3)
                    pe.wait_ge(qk_saved, b.count(2, 1))
                    value_rows(b, range(KC // 2))
                if t.within(B):
                    pe.wait_ge(prT_saved_act, t.count(2, 2))
                    pe.wait_ge(prT_saved_dve, t.count(2, 2))
                    for c in range(KC):
                        for r in range(R):
                            f = P * c + HD * r
                            last = pe.matmul(bank_o[HD * r:HD * r + HD, c, :], vs[:, t.place, f:f + HD],
                                             prT[:, r, c, :], start=True, stop=True)
                    last.then_inc(oT_ready, 1)
                b = t + 3
                if b.within(B):
                    value_rows(b, range(KC // 2, KC))
                b = t + LEAD
                if b.within(B):
                    if not (b - 1).within(B):
                        pe.wait_ge(ident_set, 2)
                    pe.wait_ge(h_normed, b.count(1, 1))
                    if (b - 1).within(B):
                        pe.wait_ge(hT_low, b.count(1))
                    for k in range(KC):
                        last = pe.transpose(bank_t[:, k, :], hn[:, b.parity, P * k:P * k + P], ident[:])
                    last.then_inc(hT_ready, 1)
                if t.within(B):
                    if not (t - 1).within(B):
                        pe.wait_ge(w_high, 4)
                        pe.wait_ge(w_low, 4)
                    pe.wait_ge(oT_low, t.count(1, 1))
                    if (t + 3).within(B):
                        pe.wait_ge(qk_saved, (t + 3).count(2, 2))
                    elif (t - 1).within(B):
                        pe.wait_ge(y_done, t.count(1))
                    product3(bank_b[:], lambda k: o_hi[:, k, :], lambda k: o_lo[:, k, :],
                             lambda k: w_hi[3][:, k, :], lambda k: w_lo[3][:, k, :]).then_inc(rows_ready, 1)

            steps(pe, step)

        @block.scalar
        def _(act):
            def exponentials(b, groups):
                for r in groups:
                    if r == 0 and not (b - 1).within(B):
                        act.wait_ge(w_low, len(W_NAMES))
                    if r == 0:
                        act.wait_ge(max_done, b.count(1, 1))
                    for c in range(KC):
                        i = KC * r + c
                        last = nc.scalar.activation(pr[:, b.parity, i, :], a[:, b.parity, i, :], ACT.Exp,
                                                    bias=negmax[:, b.parity, i:i + 1], scale=1.0,
                                                    accum_out=sums[:, b.parity, i:i + 1])
                    last.then_inc(exps, 1)

            def high_weight(i):
                act.wait_ge(w_in[i], 16)
                nc.scalar.copy(w_hi[i][:].rearrange("p c n -> p (c n)"), stage[i]).then_inc(w_high, 1)

            def step(t):
                if t.within(B):
                    exponentials(t, (2, 3))
                b = t + 3
                if b.within(B):
                    for half, bank in enumerate((bank_a, bank_b)):
                        c = 2 * b.parity + half
                        act.wait_ge(qk_ready, b.count(2, half + 1))
                        nc.scalar.copy(qk[:, b.pair_parity, c, :, :].rearrange("p i n -> p (i n)"),
                                       bank[:]).then_inc(qk_saved, 1)
                if t.within(B):
                    for r in (0, 2):
                        act.wait_ge(prT_ready, t.count(4, r + 1))
                        nc.scalar.copy(prT[:, r, :, :], quad[r][:]).then_inc(prT_saved_act, 1)
                    act.wait_ge(oT_ready, t.count(1, 1))
                    nc.scalar.copy(o_hi[:], bank_o[:]).then_inc(oT_high, 1)
                b = t + 3
                if b.within(B):
                    act.wait_ge(v_ready, b.count(1, 1))
                    nc.scalar.copy(vs[:, b.place, :], bank_a[:]).then_inc(v_saved, 1)
                b = t + LEAD
                if b.within(B):
                    act.wait_ge(hT_ready, b.count(1, 1))
                    tok = slice(b.parity * N, b.parity * N + N)
                    nc.scalar.activation(h_hi[b.pair_parity][:, :, tok], bank_t[:], ACT.Relu).then_inc(hT_high, 1)
                b = t + 1
                if b.within(B):
                    exponentials(b, (0, 1))

            steps(act, step, high_weight)

        @block.vector
        def _(dve):
            def low_weight(i):
                dve.wait_ge(w_high, i + 1)
                nc.vector.tensor_tensor(w_lo[i][:].rearrange("p c n -> p (c n)"), stage[i],
                                        w_hi[i][:].rearrange("p c n -> p (c n)").bitcast(F32),
                                        ALU.subtract).then_inc(w_low, 1)

            def reciprocals(b, part):
                cols = slice(part * HEADS // 2, (part + 1) * HEADS // 2)
                dve.wait_ge(exps, b.count(4, 2 * part + 2))
                nc.vector.reciprocal(inv[:, cols], sums[:, b.parity, cols]).then_inc(inv_done, 1)

            def live_rows_only(b, part):
                cols = slice(part * HEADS // 2, (part + 1) * HEADS // 2)
                if part == 0:
                    dve.wait_ge(abs_done, b.count(1, 1))
                dve.wait_ge(inv_done, b.count(2, part + 1))
                nc.vector.scalar_tensor_tensor(out=inv_live[:, b.parity, cols], in0=absmax[:, b.parity, cols],
                                               scalar=0.0, in1=inv[:, cols], op0=ALU.not_equal,
                                               op1=ALU.mult).then_inc(inv_live_done, 1)

            def step(t, s, half):
                def ring(b, k):
                    return xs[:, b.group % 2 if half is None else half[(s + k) // BODY % 2], b.place, :]

                b = t + LEAD
                if b.within(B):
                    dve.wait_ge(x_in[b.place], (b - b.place).count(4, 16))
                if t.within(B):
                    reciprocals(t, 1)
                if b.within(B):
                    nc.vector.bn_stats(stats[:, b.parity, :], ring(b, LEAD)).then_inc(stats_done, 1)
                    dve.wait_ge(stats_done, b.count(1, 1))
                if t.within(B):
                    live_rows_only(t, 1)
                if b.within(B):
                    nc.vector.bn_aggr(moments[:, b.parity, :], stats[:, b.parity, :]).then_inc(moments_done, 1)
                b = t + 1
                if b.within(B):
                    dve.wait_ge(scores_ready, b.count(1, 1))
                    dve.wait_ge(adj_doubled, b.count(1, 1))
                    if (b - 2).within(B):
                        dve.wait_ge(exps, (b - 2).count(4, 4))
                    for r in range(R):
                        nc.vector.scalar_tensor_tensor(
                            out=a[:, b.parity, KC * r:KC * r + KC, :], in0=quad[r][:], scalar=SCALE,
                            in1=adj2[:, b.parity:b.parity + 1, :].to_broadcast([P, KC, N]),
                            op0=ALU.mult, op1=ALU.add).then_inc(biased, 1)
                if t.within(B):
                    for r in (1, 3):
                        dve.wait_ge(prT_ready, t.count(4, r + 1))
                        nc.vector.tensor_copy(prT[:, r, :, :], quad[r][:]).then_inc(prT_saved_dve, 1)
                b = t + 1
                if b.within(B):
                    dve.wait_ge(biased, b.count(4, 4))
                    nc.vector.tensor_reduce(negmax[:, b.parity, :], a[:, b.parity, :, :], AX.X, ALU.max,
                                            negate=True).then_inc(max_done, 1)
                b = t + LEAD
                if b.within(B):
                    dve.wait_ge(rstd_done, b.count(1, 1))
                    if (b - 2).within(B):
                        dve.wait_ge(hT_ready, (b - 2).count(1, 1))
                    nc.vector.tensor_scalar(hn[:, b.parity, :], ring(b, LEAD), moments[:, b.parity, 0:1],
                                            rstd[:, b.parity, 1:2], ALU.subtract, ALU.mult).then_inc(h_normed, 1)
                if t.within(B):
                    dve.wait_ge(oT_high, t.count(1, 1))
                    nc.vector.tensor_tensor(o_lo[:], bank_o[:], o_hi[:].bitcast(F32), ALU.subtract).then_inc(oT_low, 1)
                b = t + LEAD
                if b.within(B):
                    dve.wait_ge(hT_high, b.count(1, 1))
                    tok = slice(b.parity * N, b.parity * N + N)
                    nc.vector.scalar_tensor_tensor(out=h_lo[b.pair_parity][:, :, tok], in0=bank_t[:], scalar=0.0,
                                                   in1=h_hi[b.pair_parity][:, :, tok].bitcast(F32),
                                                   op0=ALU.max, op1=ALU.subtract).then_inc(hT_low, 1)
                b = t + 1
                if b.within(B):
                    nc.vector.tensor_reduce(absmax[:, b.parity, :], a[:, b.parity, :, :], AX.X, ALU.max,
                                            apply_absolute_value=True).then_inc(abs_done, 1)
                    reciprocals(b, 0)
                    live_rows_only(b, 0)
                if t.within(B):
                    dve.wait_ge(rows_ready, t.count(1, 1))
                    if (t - 2).within(B):
                        dve.wait_ge(out_done[t.parity], (t - 2 - t.parity).count(8, 16))
                    nc.vector.tensor_tensor(y[:, t.parity, :], bank_b[:], ring(t, 0), ALU.add).then_inc(y_done, 1)

            for n in range(-LEAD, BODY * FIRST):
                if n == 2 - LEAD:
                    low_weight(0)
                    low_weight(1)
                    low_weight(2)
                if n == -1:
                    low_weight(3)
                step(Batch(0, n), n % BODY, None)
            with dve.Fori(FIRST, LAST, 1) as g:
                half = (dve.snap(g % 2), dve.snap(1 - g % 2))
                for s in range(BODY):
                    step(Batch(g, s), s, half)
            for n in range(BODY * LAST, B):
                step(Batch(0, n), n % BODY, None)

        @block.gpsimd
        def _(pool):
            nc.gpsimd.memset(ident[:], 0.0).then_inc(ident_set, 1)
            pool.wait_ge(ident_set, 1)
            nc.gpsimd.affine_select(out=ident[:], in_=ident[:], compare_op=ALU.not_equal, fill=1.0, base=0,
                                    pattern=[[-1, P]], channel_multiplier=1).then_inc(ident_set, 1)
            nc.gpsimd.memset(consts[:, 0:1], EPS).then_inc(const_set, 1)
            nc.gpsimd.memset(consts[:, 1:2], -0.5).then_inc(const_set, 1)
            pool.wait_ge(const_set, 2)

            def double_adj(b):
                pool.wait_ge(adj_in[b.place], (b - b.place).count(4, 16))
                if (b - 2).within(B):
                    pool.wait_ge(biased, (b - 2).count(4, 4))
                nc.gpsimd.tensor_tensor(adj2[:, b.parity, :], adjs[:, b.place, :], adjs[:, b.place, :],
                                        ALU.add).then_inc(adj_doubled, 1)

            def normalise(b, groups):
                for r in groups:
                    if r % 2 == 0:
                        pool.wait_ge(inv_live_done, b.count(2, r // 2 + 1))
                    heads = slice(KC * r, KC * r + KC)
                    nc.gpsimd.tensor_tensor(pr[:, b.parity, heads, :], pr[:, b.parity, heads, :],
                                            inv_live[:, b.parity, heads].unsqueeze(2).to_broadcast([P, KC, N]),
                                            ALU.mult).then_inc(normed, 1)

            def step(t):
                if t.within(B):
                    normalise(t, (2, 3))
                b = t + 2
                if b.within(B):
                    double_adj(b)
                b = t + LEAD
                if b.within(B):
                    pool.wait_ge(moments_done, b.count(1, 1))
                    nc.gpsimd.tensor_tensor(rstd[:, b.parity, 0:1], moments[:, b.parity, 1:2], consts[:, 0:1],
                                            ALU.add).then_inc(var_eps, 1)
                    pool.wait_ge(var_eps, b.count(1, 1))
                    nc.gpsimd.tensor_tensor(rstd[:, b.parity, 1:2], rstd[:, b.parity, 0:1], consts[:, 1:2],
                                            ALU.pow).then_inc(rstd_done, 1)
                b = t + 1
                if b.within(B):
                    normalise(b, (0, 1))

            steps(pool, step)


_INS = ["x", "adj", "L0_gnn_Wq", "L0_gnn_Wk", "L0_gnn_Wv", "L0_gnn_Wo"]


def kernel(**inputs):
    import numpy as np
    import concourse.bacc as bacc
    from concourse.bass_utils import run_bass_kernel_spmd

    nc = bacc.Bacc("TRN2", target_bir_lowering=False, num_devices=1)
    arrays, args = {}, []
    for name in _INS:
        a = np.asarray(inputs[name])
        a = np.ascontiguousarray(a.T if a.ndim == 2 else a)
        arrays[f"in_{name}"] = a
        args.append(nc.dram_tensor(f"in_{name}", a.shape, mybir.dt.from_np(a.dtype), kind="ExternalInput").ap())
    shape = inputs["x"].shape
    args.append(nc.dram_tensor("out_0", shape, F32, kind="ExternalOutput").ap())
    preln_graph_attention(nc, *args)
    r = run_bass_kernel_spmd(nc, [arrays], core_ids=[0])
    return r.results[0]["out_0"]
```

```python
from contextlib import ExitStack

import concourse.bass as bass
from concourse import mybir

ALU = mybir.AluOpType
ACT = mybir.ActivationFunctionType
AX = mybir.AxisListType
F32 = mybir.dt.float32
F32R = mybir.dt.float32r

P = 128
HEADS = 16
BODY = 4
LEAD = 5
EPS = 1e-5


class Batch:

    def __init__(self, base, offset):
        self.base, self.offset = base, offset
        self.ahead, self.place = divmod(offset, BODY)
        self.group = base + self.ahead

    def __add__(self, k):
        return Batch(self.base, self.offset + k)

    def __sub__(self, k):
        return Batch(self.base, self.offset - k)

    def count(self, per_batch, more=0):
        return self.base * (BODY * per_batch) + (self.offset * per_batch + more)

    def within(self, n):
        return not isinstance(self.base, int) or 0 <= BODY * self.base + self.offset < n

    @property
    def parity(self):
        return self.place % 2

    @property
    def pair_parity(self):
        return self.place // 2

    @property
    def of_pair(self):
        return self - self.parity

    @property
    def of_group(self):
        return self - self.place


def preln_graph_attention(nc, x, adj, wqT, wkT, wvT, woT, out):
    B, N, D = x.shape
    assert N == P and D % P == 0 and B % BODY == 0
    HD = D // HEADS
    KC = D // P
    R = P // HD
    assert HEADS == R * KC
    SCALE = float(D) ** -0.5
    PAIR = 2 * N
    BLK = 32
    Q = N // BLK
    MOVES = [(i, j) for i in range(Q) for j in range(Q)]
    MOVED = 16 * len(MOVES)
    FIRST, LAST = 1, B // BODY - 2

    ctx = ExitStack()

    def sb(name, shape, dt=F32):
        return ctx.enter_context(nc.sbuf_tensor(name, shape, dt))

    def sem(name):
        return ctx.enter_context(nc.semaphore(name))

    x_of = x.rearrange("(g s) n d -> g s n d", s=BODY)
    adj_of = adj.rearrange("(g s) n m -> g s n m", s=BODY)
    out_of = out.rearrange("(g s) n d -> g s n d", s=BODY)

    with ctx:
        W_NAMES = ("q", "k", "v", "o")
        w_hi = [sb(f"w_hi_{n}", [P, KC, D], F32R) for n in W_NAMES]
        w_lo = [sb(f"w_lo_{n}", [P, KC, D], F32R) for n in W_NAMES]
        xs = sb("xs", [P, 2, BODY, D])
        adjs = sb("adjs", [P, BODY, N])
        adj2 = sb("adj2", [P, 2, N])
        stats = sb("stats", [P, 2, 6])
        moments = sb("moments", [P, 2, 2])
        rstd = sb("rstd", [P, 2, 2])
        hn = sb("hn", [P, 2, D])
        h_hi = [sb(f"h_hi{i}", [P, KC, PAIR], F32R) for i in range(2)]
        h_lo = [sb(f"h_lo{i}", [P, KC, PAIR], F32R) for i in range(2)]
        qk = sb("qk", [P, 2, KC, 2, PAIR])
        vs = sb("vs", [P, BODY, D])
        a = sb("a", [P, HEADS, N])
        pr = sb("pr", [P, HEADS, N])
        blocks = [sb(f"blocks{i}", [P, Q, HEADS, BLK]) for i in range(2)]
        prT = [sb(f"prT{i}", [P, Q, HEADS, BLK]) for i in range(2)]
        negmax = sb("negmax", [P, 2, HEADS])
        absmax = sb("absmax", [P, 2, HEADS])
        sums = sb("sums", [P, 2, HEADS])
        inv = sb("inv", [P, HEADS])
        inv_live = sb("inv_live", [P, 2, HEADS])
        o_hi = sb("o_hi", [P, KC, N], F32R)
        o_lo = sb("o_lo", [P, KC, N], F32R)
        y = sb("y", [P, 2, D])
        ident = sb("ident", [P, P])
        consts = sb("consts", [P, 2])
        stage = [pr[:].rearrange("p h n -> p (h n)"), a[:].rearrange("p h n -> p (h n)"),
                 blocks[0][:].rearrange("p j h n -> p (j h n)"), prT[0][:].rearrange("p i h n -> p (i h n)")]

        quad = [ctx.enter_context(nc.psum_tensor(f"quad{r}", [P, KC, N], F32)) for r in range(R)]
        bank_a = ctx.enter_context(nc.psum_tensor("bank_a", [P, D], F32))
        bank_b = ctx.enter_context(nc.psum_tensor("bank_b", [P, D], F32))
        bank_c = ctx.enter_context(nc.psum_tensor("bank_c", [P, D], F32))
        bank_o = ctx.enter_context(nc.psum_tensor("bank_o", [P, KC, N], F32))
        bank_t = bank_b[:].rearrange("p (c n) -> p c n", c=KC)

        w_in = [sem(f"w_in{i}") for i in range(4)]
        w_high = sem("w_high")
        w_low = sem("w_low")
        x_in = [sem(f"x_in{i}") for i in range(BODY)]
        adj_in = [sem(f"adj_in{i}") for i in range(BODY)]
        out_done = [sem(f"out_done{i}") for i in range(2)]
        ident_set = sem("ident_set")
        const_set = sem("const_set")
        scores_ready = sem("scores_ready")
        qk_ready = sem("qk_ready")
        v_ready = sem("v_ready")
        oT_ready = sem("oT_ready")
        rows_ready = sem("rows_ready")
        hT_ready = sem("hT_ready")
        qk_saved = sem("qk_saved")
        v_saved = sem("v_saved")
        oT_high = sem("oT_high")
        hT_high = sem("hT_high")
        exps = sem("exps")
        stats_done = sem("stats_done")
        moments_done = sem("moments_done")
        h_normed = sem("h_normed")
        biased = sem("biased")
        max_done = sem("max_done")
        abs_done = sem("abs_done")
        inv_done = sem("inv_done")
        inv_live_done = sem("inv_live_done")
        blocks_turned = sem("blocks_turned")
        oT_low = sem("oT_low")
        hT_low = sem("hT_low")
        y_done = sem("y_done")
        blocks_moved = [sem(f"blocks_moved{i}") for i in range(2)]
        adj_doubled = sem("adj_doubled")
        var_eps = sem("var_eps")
        rstd_done = sem("rstd_done")
        normed = sem("normed")

        block = ctx.enter_context(nc.Block())

        def x_ring(b, halves):
            return xs[:, halves[b.ahead % 2], b.place, :]

        def steps(eng, step, first=-LEAD, output_weight=None, uses_x_ring=False):
            for n in range(first, BODY * FIRST):
                if output_weight and n == -1:
                    output_weight(3)
                step(Batch(0, n), (0, 1))
            with eng.Fori(FIRST, LAST, 1) as g:
                halves = (eng.snap(g % 2), eng.snap(1 - g % 2)) if uses_x_ring else None
                for s in range(BODY):
                    step(Batch(g, s), halves)
            for n in range(BODY * LAST, B + 1):
                step(Batch(0, n), (0, 1))

        @block.sync
        def _(sp):
            def load_weight(i, src):
                sp.dma_start(stage[i].rearrange("p (c n) -> p c n", c=KC),
                             src.rearrange("(c p) n -> p c n", p=P)).then_inc(w_in[i], 16)

            def load_x(b, halves=(0, 1)):
                sp.dma_start(x_ring(b, halves), x_of[b.group, b.place]).then_inc(x_in[b.place], 16)

            def load_adj(b):
                sp.dma_start(adjs[:, b.place, :], adj_of[b.group, b.place]).then_inc(adj_in[b.place], 16)

            load_x(Batch(0, 0))
            load_x(Batch(0, 1))
            load_weight(0, wqT)
            load_weight(1, wkT)
            load_x(Batch(0, 2))
            load_x(Batch(0, 3))
            load_weight(2, wvT)
            for n in range(BODY):
                load_adj(Batch(0, n))
            load_weight(3, woT)
            for n in range(BODY, 2 * BODY):
                sp.wait_ge(stats_done, n - BODY + 1)
                load_x(Batch(0, n))
            for n in range(BODY, BODY + 2):
                sp.wait_ge(adj_doubled, n - BODY + 1)
                load_adj(Batch(0, n))

            def step(t, halves):
                if t.within(B):
                    sp.wait_ge(blocks_turned, t.count(2, 2))
                    if (t - 2).within(B):
                        sp.wait_ge(oT_ready, (t - 1).count(1))
                    for i, j in MOVES:
                        sp.dma_start(prT[t.parity][BLK * j:BLK * j + BLK, i, :, :],
                                     blocks[t.parity][BLK * i:BLK * i + BLK, j, :, :]
                                     ).then_inc(blocks_moved[t.parity], 16)
                u = t - 1
                if u.within(B):
                    sp.wait_ge(y_done, u.count(1, 1))
                    sp.dma_start(out_of[u.group, u.place], y[:, u.parity, :]).then_inc(out_done[u.parity], 16)
                    b = u + 2 * BODY
                    if b.within(B):
                        load_x(b, halves)
                b = t + (BODY + 2)
                if t.within(B) and b.within(B):
                    sp.wait_ge(adj_doubled, (b - BODY).count(1, 1))
                    load_adj(b)

            steps(sp, step, uses_x_ring=True)
            sp.wait_ge(out_done[0], 16 * (B // 2))
            sp.wait_ge(out_done[1], 16 * (B // 2))

        @block.tensor
        def _(pe):
            def product3(dst, hi_l, lo_l, hi_r, lo_r, chunks=range(KC)):
                for k in chunks:
                    pe.matmul(dst, hi_l(k), hi_r(k), start=(k == 0), stop=False)
                    pe.matmul(dst, hi_l(k), lo_r(k), start=False, stop=False)
                    last = pe.matmul(dst, lo_l(k), hi_r(k), start=False, stop=(k == KC - 1))
                return last

            def scores(b, chunks):
                if 0 in chunks:
                    pe.wait_ge(qk_saved, b.of_pair.count(2, 4))
                if 0 in chunks and (b - 1).within(B):
                    pe.wait_ge(biased, b.count(4))
                tok = slice(b.parity * N, b.parity * N + N)
                for c in chunks:
                    for r in range(R):
                        rows = slice(HD * r, HD * r + HD)
                        last = pe.matmul(quad[r][:, c, :], qk[rows, b.pair_parity, c, 0, tok],
                                         qk[rows, b.pair_parity, c, 1, tok], start=True, stop=True)
                if KC - 1 in chunks:
                    last.then_inc(scores_ready, 1)

            def qk_chunk(b, half, bank):
                c = 2 * b.parity + half
                hi, lo = h_hi[b.pair_parity], h_lo[b.pair_parity]
                cols = slice(P * c, P * c + P)
                for i in range(2):
                    if half == 0 and not (b - 1).within(B):
                        pe.wait_ge(w_low, i + 1)
                    last = product3(bank[:, i * PAIR:(i + 1) * PAIR],
                                    lambda k: w_hi[i][:, k, cols], lambda k: w_lo[i][:, k, cols],
                                    lambda k: hi[:, k, :], lambda k: lo[:, k, :])
                last.then_inc(qk_ready, 1)

            def step(t, _):
                b = t + 1
                if b.within(B):
                    scores(b, range(KC // 2) if (t + 3).within(B) else range(KC))
                u = t - 1
                b = t + 3
                if b.within(B):
                    pe.wait_ge(hT_low, b.of_pair.count(1, 2))
                    if (u - 1).within(B):
                        pe.wait_ge(y_done, u.count(1))
                    elif (b - 1).within(B):
                        pe.wait_ge(qk_saved, b.count(2, -1))
                    qk_chunk(b, 0, bank_a)
                if u.within(B):
                    pe.wait_ge(blocks_moved[u.parity], (u - u.parity).count(MOVED // 2, MOVED))
                    for c in range(KC):
                        for r in range(R):
                            f = P * c + HD * r
                            last = pe.matmul(bank_o[HD * r:HD * r + HD, c, :], vs[:, u.place, f:f + HD],
                                             prT[u.parity][:, :, KC * r + c, :], start=True, stop=True)
                    last.then_inc(oT_ready, 1)
                b = t + 1
                if b.within(B) and (t + 3).within(B):
                    scores(b, range(KC // 2, KC))
                b = t + 3
                if b.within(B):
                    if (t + LEAD - 1).within(B):
                        pe.wait_ge(hT_low, t.count(1, LEAD))
                    elif (b - 1).within(B):
                        pe.wait_ge(qk_saved, b.count(2))
                    qk_chunk(b, 1, bank_b)
                if u.within(B):
                    if not (u - 1).within(B):
                        pe.wait_ge(w_low, 4)
                    pe.wait_ge(oT_low, u.count(1, 1))
                    if (t + 3).within(B):
                        pe.wait_ge(qk_saved, (t + 3).count(2, 1))
                    else:
                        pe.wait_ge(y_done, u.count(1))
                    product3(bank_a[:], lambda k: o_hi[:, k, :], lambda k: o_lo[:, k, :],
                             lambda k: w_hi[3][:, k, :], lambda k: w_lo[3][:, k, :]).then_inc(rows_ready, 1)
                b = t + LEAD
                if b.within(B):
                    if not (b - 1).within(B):
                        pe.wait_ge(ident_set, 2)
                    pe.wait_ge(h_normed, b.count(1, 1))
                    if (t + 3).within(B):
                        pe.wait_ge(qk_saved, (t + 3).count(2, 2))
                    elif (b - 1).within(B):
                        pe.wait_ge(hT_low, b.count(1))
                    for k in range(KC):
                        last = pe.transpose(bank_t[:, k, :], hn[:, b.parity, P * k:P * k + P], ident[:])
                    last.then_inc(hT_ready, 1)
                b = t + 3
                if b.within(B):
                    if (b - 1).within(B):
                        pe.wait_ge(v_saved, b.count(1))
                    else:
                        pe.wait_ge(w_low, 3)
                    hi, lo = h_hi[b.pair_parity], h_lo[b.pair_parity]
                    tok = slice(b.parity * N, b.parity * N + N)
                    product3(bank_c[:], lambda k: hi[:, k, tok], lambda k: lo[:, k, tok],
                             lambda k: w_hi[2][:, k, :], lambda k: w_lo[2][:, k, :]).then_inc(v_ready, 1)

            steps(pe, step)

        @block.scalar
        def _(act):
            def exponentials(b, groups):
                for r in groups:
                    if r == 0 and not (b - 1).within(B):
                        act.wait_ge(w_low, len(W_NAMES))
                    if r == 0 and (b - 1).within(B):
                        act.wait_ge(blocks_turned, b.count(2))
                    if r % 2 == 0:
                        act.wait_ge(max_done, b.count(2, r // 2 + 1))
                    for c in range(KC):
                        i = KC * r + c
                        last = nc.scalar.activation(pr[:, i, :], a[:, i, :], ACT.Exp,
                                                    bias=negmax[:, b.parity, i:i + 1], scale=1.0,
                                                    accum_out=sums[:, b.parity, i:i + 1])
                    last.then_inc(exps, 1)

            def save_qk(b, half, bank):
                c = 2 * b.parity + half
                act.wait_ge(qk_ready, b.count(2, half + 1))
                nc.scalar.copy(qk[:, b.pair_parity, c, :, :].rearrange("p i n -> p (i n)"),
                               bank[:]).then_inc(qk_saved, 1)

            def high_hT(b):
                act.wait_ge(hT_ready, b.count(1, 1))
                tok = slice(b.parity * N, b.parity * N + N)
                nc.scalar.activation(h_hi[b.pair_parity][:, :, tok], bank_t, ACT.Relu).then_inc(hT_high, 1)

            def high_weight(i):
                act.wait_ge(w_in[i], 16)
                nc.scalar.copy(w_hi[i][:].rearrange("p c n -> p (c n)"), stage[i]).then_inc(w_high, 1)

            def step(t, _):
                if t.within(B):
                    exponentials(t, (3,))
                b = t + 2
                if b.within(B):
                    act.wait_ge(v_ready, b.count(1, 1))
                    nc.scalar.copy(vs[:, b.place, :], bank_c[:]).then_inc(v_saved, 1)
                b = t + 3
                if b.within(B):
                    save_qk(b, 0, bank_a)
                u = t - 1
                if u.within(B):
                    act.wait_ge(oT_ready, u.count(1, 1))
                    nc.scalar.copy(o_hi[:], bank_o[:]).then_inc(oT_high, 1)
                b = t + 3
                if b.within(B):
                    save_qk(b, 1, bank_b)
                b = t + 1
                if b.within(B):
                    exponentials(b, (0, 1))
                if (t + LEAD).within(B):
                    high_hT(t + LEAD)
                b = t + 1
                if b.within(B):
                    exponentials(b, (2,))

            high_hT(Batch(0, 0))
            high_weight(0)
            high_hT(Batch(0, 1))
            high_weight(1)
            high_weight(2)
            steps(act, step, first=2 - LEAD, output_weight=high_weight)

        @block.vector
        def _(dve):
            def low_weight(i):
                dve.wait_ge(w_high, i + 1)
                nc.vector.tensor_tensor(w_lo[i][:].rearrange("p c n -> p (c n)"), stage[i],
                                        w_hi[i][:].rearrange("p c n -> p (c n)").bitcast(F32),
                                        ALU.subtract).then_inc(w_low, 1)

            def statistics(b, halves):
                nc.vector.bn_stats(stats[:, b.parity, :], x_ring(b, halves)).then_inc(stats_done, 1)

            def aggregate(b):
                nc.vector.bn_aggr(moments[:, b.parity, :], stats[:, b.parity, :]).then_inc(moments_done, 1)

            def norm_rows(b, halves):
                dve.wait_ge(rstd_done, b.count(1, 1))
                if (b - 2).within(B):
                    dve.wait_ge(hT_ready, (b - 2).count(1, 1))
                nc.vector.tensor_scalar(hn[:, b.parity, :], x_ring(b, halves), moments[:, b.parity, 0:1],
                                        rstd[:, b.parity, 1:2], ALU.subtract, ALU.mult).then_inc(h_normed, 1)

            def low_hT(b):
                dve.wait_ge(hT_high, b.count(1, 1))
                tok = slice(b.parity * N, b.parity * N + N)
                nc.vector.scalar_tensor_tensor(out=h_lo[b.pair_parity][:, :, tok], in0=bank_t, scalar=0.0,
                                               in1=h_hi[b.pair_parity][:, :, tok].bitcast(F32),
                                               op0=ALU.max, op1=ALU.subtract).then_inc(hT_low, 1)

            def reciprocals(b, part):
                cols = slice(part * HEADS // 2, (part + 1) * HEADS // 2)
                dve.wait_ge(exps, b.count(4, 2 * part + 2))
                nc.vector.reciprocal(inv[:, cols], sums[:, b.parity, cols]).then_inc(inv_done, 1)

            def live_rows_only(b, part):
                cols = slice(part * HEADS // 2, (part + 1) * HEADS // 2)
                dve.wait_ge(abs_done, b.count(2, part + 1))
                dve.wait_ge(inv_done, b.count(2, part + 1))
                nc.vector.scalar_tensor_tensor(out=inv_live[:, b.parity, cols], in0=absmax[:, b.parity, cols],
                                               scalar=0.0, in1=inv[:, cols], op0=ALU.not_equal,
                                               op1=ALU.mult).then_inc(inv_live_done, 1)

            def turn_blocks(b, part):
                heads = slice(part * HEADS // 2, (part + 1) * HEADS // 2)
                dve.wait_ge(normed, b.count(4, 2 * part + 2))
                if part == 0 and (b - 2).within(B):
                    dve.wait_ge(blocks_moved[b.parity], (b - 2 - b.parity).count(MOVED // 2, MOVED))
                nc.vector.transpose(blocks[b.parity][:, :, heads, :].rearrange("p j h q -> p h j q"),
                                    pr[:, heads, :].rearrange("p h (j m) -> p h j m", j=Q)).then_inc(blocks_turned, 1)

            def biased_max(b, part):
                if part == 0:
                    dve.wait_ge(scores_ready, b.count(1, 1))
                    dve.wait_ge(adj_doubled, b.count(1, 1))
                    if (b - 1).within(B):
                        dve.wait_ge(exps, b.count(4))
                for r in (2 * part, 2 * part + 1):
                    nc.vector.scalar_tensor_tensor(
                        out=a[:, KC * r:KC * r + KC, :], in0=quad[r][:], scalar=SCALE,
                        in1=adj2[:, b.parity:b.parity + 1, :].to_broadcast([P, KC, N]),
                        op0=ALU.mult, op1=ALU.add).then_inc(biased, 1)
                heads = slice(part * HEADS // 2, (part + 1) * HEADS // 2)
                dve.wait_ge(biased, b.count(4, 2 * part + 2))
                nc.vector.tensor_reduce(negmax[:, b.parity, heads], a[:, heads, :], AX.X, ALU.max,
                                        negate=True).then_inc(max_done, 1)

            def row_absmax(b, part):
                heads = slice(part * HEADS // 2, (part + 1) * HEADS // 2)
                nc.vector.tensor_reduce(absmax[:, b.parity, heads], a[:, heads, :], AX.X, ALU.max,
                                        apply_absolute_value=True).then_inc(abs_done, 1)

            def step(t, halves):
                b = t + LEAD
                if t.within(B):
                    turn_blocks(t, 0)
                if b.within(B):
                    dve.wait_ge(x_in[b.place], b.of_group.count(4, 16))
                if t.within(B):
                    reciprocals(t, 1)
                if b.within(B):
                    statistics(b, halves)
                    dve.wait_ge(stats_done, b.count(1, 1))
                if t.within(B):
                    live_rows_only(t, 1)
                if b.within(B):
                    aggregate(b)
                early = not (t + 3).within(B)
                b = t + 1
                if b.within(B) and early:
                    biased_max(b, 0)
                if t.within(B):
                    turn_blocks(t, 1)
                b = t + LEAD
                if b.within(B):
                    norm_rows(b, halves)
                u = t - 1
                if u.within(B):
                    dve.wait_ge(oT_high, u.count(1, 1))
                    nc.vector.tensor_tensor(o_lo[:], bank_o[:], o_hi[:].bitcast(F32), ALU.subtract).then_inc(oT_low, 1)
                b = t + 1
                if b.within(B):
                    if not early:
                        biased_max(b, 0)
                    biased_max(b, 1)
                    row_absmax(b, 0)
                    reciprocals(b, 0)
                    live_rows_only(b, 0)
                    row_absmax(b, 1)
                if u.within(B):
                    dve.wait_ge(rows_ready, u.count(1, 1))
                    if (u - 2).within(B):
                        dve.wait_ge(out_done[u.parity], (u - 2 - u.parity).count(8, 16))
                    nc.vector.tensor_tensor(y[:, u.parity, :], bank_a[:], x_ring(u, halves), ALU.add).then_inc(y_done, 1)
                if (t + LEAD).within(B):
                    low_hT(t + LEAD)

            first, second = Batch(0, 0), Batch(0, 1)
            for b in (first, second):
                dve.wait_ge(x_in[b.place], 16)
                statistics(b, (0, 1))
                dve.wait_ge(stats_done, b.count(1, 1))
                aggregate(b)
            norm_rows(first, (0, 1))
            norm_rows(second, (0, 1))
            low_hT(first)
            low_weight(0)
            low_hT(second)
            low_weight(1)
            low_weight(2)
            steps(dve, step, first=2 - LEAD, output_weight=low_weight, uses_x_ring=True)

        @block.gpsimd
        def _(pool):
            nc.gpsimd.memset(ident[:], 0.0).then_inc(ident_set, 1)
            pool.wait_ge(ident_set, 1)
            nc.gpsimd.affine_select(out=ident[:], in_=ident[:], compare_op=ALU.not_equal, fill=1.0, base=0,
                                    pattern=[[-1, P]], channel_multiplier=1).then_inc(ident_set, 1)
            nc.gpsimd.memset(consts[:, 0:1], EPS).then_inc(const_set, 1)
            nc.gpsimd.memset(consts[:, 1:2], -0.5).then_inc(const_set, 1)
            pool.wait_ge(const_set, 2)

            def double_adj(b):
                pool.wait_ge(adj_in[b.place], b.of_group.count(4, 16))
                if (b - 2).within(B):
                    pool.wait_ge(biased, (b - 2).count(4, 4))
                nc.gpsimd.tensor_tensor(adj2[:, b.parity, :], adjs[:, b.place, :], adjs[:, b.place, :],
                                        ALU.add).then_inc(adj_doubled, 1)

            def normalise(b, groups):
                for r in groups:
                    if r % 2 == 0:
                        pool.wait_ge(inv_live_done, b.count(2, r // 2 + 1))
                    heads = slice(KC * r, KC * r + KC)
                    nc.gpsimd.tensor_tensor(pr[:, heads, :], pr[:, heads, :],
                                            inv_live[:, b.parity, heads].unsqueeze(2).to_broadcast([P, KC, N]),
                                            ALU.mult).then_inc(normed, 1)

            def step(t, _):
                if t.within(B):
                    normalise(t, (2, 3))
                b = t + LEAD
                if b.within(B):
                    pool.wait_ge(moments_done, b.count(1, 1))
                    nc.gpsimd.tensor_tensor(rstd[:, b.parity, 0:1], moments[:, b.parity, 1:2], consts[:, 0:1],
                                            ALU.add).then_inc(var_eps, 1)
                    pool.wait_ge(var_eps, b.count(1, 1))
                    nc.gpsimd.tensor_tensor(rstd[:, b.parity, 1:2], rstd[:, b.parity, 0:1], consts[:, 1:2],
                                            ALU.pow).then_inc(rstd_done, 1)
                b = t + 2
                if b.within(B):
                    double_adj(b)
                b = t + 1
                if b.within(B):
                    normalise(b, (0, 1))

            steps(pool, step)


_INS = ["x", "adj", "L0_gnn_Wq", "L0_gnn_Wk", "L0_gnn_Wv", "L0_gnn_Wo"]


def kernel(**inputs):
    import numpy as np
    import concourse.bacc as bacc
    from concourse.bass_utils import run_bass_kernel_spmd

    nc = bacc.Bacc("TRN2", target_bir_lowering=False, num_devices=1)
    arrays, args = {}, []
    for name in _INS:
        a = np.asarray(inputs[name])
        a = np.ascontiguousarray(a.T if a.ndim == 2 else a)
        arrays[f"in_{name}"] = a
        args.append(nc.dram_tensor(f"in_{name}", a.shape, mybir.dt.from_np(a.dtype), kind="ExternalInput").ap())
    shape = inputs["x"].shape
    args.append(nc.dram_tensor("out_0", shape, F32, kind="ExternalOutput").ap())
    preln_graph_attention(nc, *args)
    r = run_bass_kernel_spmd(nc, [arrays], core_ids=[0])
    return r.results[0]["out_0"]
```

```python
from contextlib import ExitStack

import concourse.bass as bass
from concourse import mybir

ALU = mybir.AluOpType
ACT = mybir.ActivationFunctionType
AX = mybir.AxisListType
F32 = mybir.dt.float32
F32R = mybir.dt.float32r

P = 128
HEADS = 16
BODY = 4
LEAD = 5
DRAIN = 3
EPS = 1e-5


class Batch:

    def __init__(self, base, offset):
        self.base, self.offset = base, offset
        self.ahead, self.place = divmod(offset, BODY)
        self.group = base + self.ahead

    def __add__(self, k):
        return Batch(self.base, self.offset + k)

    def __sub__(self, k):
        return Batch(self.base, self.offset - k)

    def count(self, per_batch, more=0):
        return self.base * (BODY * per_batch) + (self.offset * per_batch + more)

    def within(self, n):
        return not isinstance(self.base, int) or 0 <= BODY * self.base + self.offset < n

    def drained(self, n):
        if not isinstance(self.base, int) or BODY * self.base + self.offset < n - DRAIN:
            return None
        return BODY * self.base + self.offset - (n - DRAIN)

    @property
    def parity(self):
        return self.place % 2

    @property
    def pair_parity(self):
        return self.place // 2

    @property
    def of_pair(self):
        return self - self.parity

    @property
    def of_group(self):
        return self - self.place


def preln_graph_attention(nc, x, adj, wqT, wkT, wvT, woT, out):
    B, N, D = x.shape
    assert N == P and D % P == 0 and B % BODY == 0
    HD = D // HEADS
    KC = D // P
    R = P // HD
    assert HEADS == R * KC
    SCALE = float(D) ** -0.5
    PAIR = 2 * N
    BLK = 32
    Q = N // BLK
    MOVES = [(i, j) for i in range(Q) for j in range(Q)]
    MOVED = 16 * len(MOVES)
    FIRST, LAST = 1, B // BODY - 2

    ctx = ExitStack()

    def sb(name, shape, dt=F32):
        return ctx.enter_context(nc.sbuf_tensor(name, shape, dt))

    def sem(name):
        return ctx.enter_context(nc.semaphore(name))

    x_of = x.rearrange("(g s) n d -> g s n d", s=BODY)
    adj_of = adj.rearrange("(g s) n m -> g s n m", s=BODY)
    out_of = out.rearrange("(g s) n d -> g s n d", s=BODY)

    with ctx:
        W_NAMES = ("q", "k", "v", "o")
        w_hi = [sb(f"w_hi_{n}", [P, KC, D], F32R) for n in W_NAMES]
        w_lo = [sb(f"w_lo_{n}", [P, KC, D], F32R) for n in W_NAMES]
        xs = sb("xs", [P, 2, BODY, D])
        adjs = sb("adjs", [P, BODY, N])
        adj2 = sb("adj2", [P, 2, N])
        stats = sb("stats", [P, 2, 6])
        moments = sb("moments", [P, 2, 2])
        rstd = sb("rstd", [P, 2, 2])
        hn = sb("hn", [P, 2, D])
        h_hi = [sb(f"h_hi{i}", [P, KC, PAIR], F32R) for i in range(2)]
        h_lo = [sb(f"h_lo{i}", [P, KC, PAIR], F32R) for i in range(2)]
        qk = sb("qk", [P, 2, KC, 2, PAIR])
        vs = sb("vs", [P, BODY, D])
        a = sb("a", [P, HEADS, N])
        pr = sb("pr", [P, HEADS, N])
        blocks = [sb(f"blocks{i}", [P, Q, HEADS, BLK]) for i in range(2)]
        prT = [sb(f"prT{i}", [P, Q, HEADS, BLK]) for i in range(2)]
        negmax = sb("negmax", [P, 2, HEADS])
        absmax = sb("absmax", [P, 2, HEADS])
        sums = sb("sums", [P, 2, HEADS])
        inv = sb("inv", [P, HEADS])
        inv_live = sb("inv_live", [P, 2, HEADS])
        o_hi = sb("o_hi", [P, KC, N], F32R)
        o_lo = sb("o_lo", [P, KC, N], F32R)
        y = sb("y", [P, 2, D])
        ident = sb("ident", [P, P])
        consts = sb("consts", [P, 2])
        stage = [pr[:].rearrange("p h n -> p (h n)"), a[:].rearrange("p h n -> p (h n)"),
                 blocks[0][:].rearrange("p j h n -> p (j h n)"), prT[0][:].rearrange("p i h n -> p (i h n)")]

        quad = [ctx.enter_context(nc.psum_tensor(f"quad{r}", [P, KC, N], F32)) for r in range(R)]
        bank_a = ctx.enter_context(nc.psum_tensor("bank_a", [P, D], F32))
        bank_b = ctx.enter_context(nc.psum_tensor("bank_b", [P, D], F32))
        bank_c = ctx.enter_context(nc.psum_tensor("bank_c", [P, D], F32))
        bank_o = ctx.enter_context(nc.psum_tensor("bank_o", [P, KC, N], F32))
        bank_t = bank_b[:].rearrange("p (c n) -> p c n", c=KC)
        pT_banks = [bank_t, bank_c[:].rearrange("p (c n) -> p c n", c=KC)]

        w_in = [sem(f"w_in{i}") for i in range(4)]
        w_high = sem("w_high")
        w_low = sem("w_low")
        x_in = [sem(f"x_in{i}") for i in range(BODY)]
        adj_in = [sem(f"adj_in{i}") for i in range(BODY)]
        out_done = [sem(f"out_done{i}") for i in range(2)]
        ident_set = sem("ident_set")
        const_set = sem("const_set")
        scores_ready = sem("scores_ready")
        qk_ready = sem("qk_ready")
        v_ready = sem("v_ready")
        oT_ready = sem("oT_ready")
        rows_ready = sem("rows_ready")
        hT_ready = sem("hT_ready")
        qk_saved = sem("qk_saved")
        v_saved = sem("v_saved")
        oT_high = sem("oT_high")
        hT_high = sem("hT_high")
        exps = sem("exps")
        normed_last = sem("normed_last")
        pT_ready = sem("pT_ready")
        pT_saved = [sem("pT_saved_act"), sem("pT_saved_dve")]
        stats_done = sem("stats_done")
        moments_done = sem("moments_done")
        h_normed = sem("h_normed")
        biased = sem("biased")
        max_done = sem("max_done")
        abs_done = sem("abs_done")
        inv_done = sem("inv_done")
        inv_live_done = sem("inv_live_done")
        blocks_turned = sem("blocks_turned")
        oT_low = sem("oT_low")
        hT_low = sem("hT_low")
        y_done = sem("y_done")
        blocks_moved = [sem(f"blocks_moved{i}") for i in range(2)]
        adj_doubled = sem("adj_doubled")
        var_eps = sem("var_eps")
        rstd_done = sem("rstd_done")
        normed = sem("normed")

        block = ctx.enter_context(nc.Block())

        def x_ring(b, halves):
            return xs[:, halves[b.ahead % 2], b.place, :]

        def steps(eng, step, drain, first=-LEAD, output_weight=None, uses_x_ring=False):
            for n in range(first, BODY * FIRST):
                if output_weight and n == -1:
                    output_weight(3)
                step(Batch(0, n), (0, 1))
            with eng.Fori(FIRST, LAST, 1) as g:
                halves = (eng.snap(g % 2), eng.snap(1 - g % 2)) if uses_x_ring else None
                for s in range(BODY):
                    step(Batch(g, s), halves)
            for n in range(BODY * LAST, B - DRAIN):
                step(Batch(0, n), (0, 1))
            for n in range(B - DRAIN, B):
                drain(Batch(0, n))

        @block.sync
        def _(sp):
            def load_weight(i, src):
                sp.dma_start(stage[i].rearrange("p (c n) -> p c n", c=KC),
                             src.rearrange("(c p) n -> p c n", p=P)).then_inc(w_in[i], 16)

            def load_x(b, halves=(0, 1)):
                sp.dma_start(x_ring(b, halves), x_of[b.group, b.place]).then_inc(x_in[b.place], 16)

            def load_adj(b):
                sp.dma_start(adjs[:, b.place, :], adj_of[b.group, b.place]).then_inc(adj_in[b.place], 16)

            def store(u):
                sp.wait_ge(y_done, u.count(1, 1))
                sp.dma_start(out_of[u.group, u.place], y[:, u.parity, :]).then_inc(out_done[u.parity], 16)

            load_x(Batch(0, 0))
            load_x(Batch(0, 1))
            load_weight(0, wqT)
            load_weight(1, wkT)
            load_x(Batch(0, 2))
            load_x(Batch(0, 3))
            load_weight(2, wvT)
            for n in range(BODY):
                load_adj(Batch(0, n))
            load_weight(3, woT)
            for n in range(BODY, 2 * BODY):
                sp.wait_ge(stats_done, n - BODY + 1)
                load_x(Batch(0, n))
            for n in range(BODY, BODY + 2):
                sp.wait_ge(adj_doubled, n - BODY + 1)
                load_adj(Batch(0, n))

            def step(t, halves):
                if t.within(B):
                    sp.wait_ge(blocks_turned, t.count(2, 2))
                    if (t - 2).within(B):
                        sp.wait_ge(oT_ready, (t - 1).count(1))
                    for i, j in MOVES:
                        sp.dma_start(prT[t.parity][BLK * j:BLK * j + BLK, i, :, :],
                                     blocks[t.parity][BLK * i:BLK * i + BLK, j, :, :]
                                     ).then_inc(blocks_moved[t.parity], 16)
                u = t - 1
                if u.within(B):
                    store(u)
                    b = u + 2 * BODY
                    if b.within(B):
                        load_x(b, halves)
                b = t + (BODY + 2)
                if t.within(B) and b.within(B):
                    sp.wait_ge(adj_doubled, (b - BODY).count(1, 1))
                    load_adj(b)

            def drain(t):
                if t.drained(B) == 0:
                    store(t - 1)
                store(t)

            steps(sp, step, drain, uses_x_ring=True)
            sp.wait_ge(out_done[0], 16 * (B // 2))
            sp.wait_ge(out_done[1], 16 * (B // 2))

        @block.tensor
        def _(pe):
            def product3(dst, hi_l, lo_l, hi_r, lo_r, chunks=range(KC)):
                for k in chunks:
                    pe.matmul(dst, hi_l(k), hi_r(k), start=(k == 0), stop=False)
                    pe.matmul(dst, hi_l(k), lo_r(k), start=False, stop=False)
                    last = pe.matmul(dst, lo_l(k), hi_r(k), start=False, stop=(k == KC - 1))
                return last

            def scores(b, chunks):
                if 0 in chunks:
                    pe.wait_ge(qk_saved, b.of_pair.count(2, 4))
                if 0 in chunks and (b - 1).within(B):
                    pe.wait_ge(biased, b.count(4))
                tok = slice(b.parity * N, b.parity * N + N)
                for c in chunks:
                    for r in range(R):
                        rows = slice(HD * r, HD * r + HD)
                        last = pe.matmul(quad[r][:, c, :], qk[rows, b.pair_parity, c, 0, tok],
                                         qk[rows, b.pair_parity, c, 1, tok], start=True, stop=True)
                if KC - 1 in chunks:
                    last.then_inc(scores_ready, 1)

            def qk_chunk(b, half, bank):
                c = 2 * b.parity + half
                hi, lo = h_hi[b.pair_parity], h_lo[b.pair_parity]
                cols = slice(P * c, P * c + P)
                for i in range(2):
                    if half == 0 and not (b - 1).within(B):
                        pe.wait_ge(w_low, i + 1)
                    last = product3(bank[:, i * PAIR:(i + 1) * PAIR],
                                    lambda k: w_hi[i][:, k, cols], lambda k: w_lo[i][:, k, cols],
                                    lambda k: hi[:, k, :], lambda k: lo[:, k, :])
                last.then_inc(qk_ready, 1)

            def transposed_output(u):
                if u.drained(B) is None:
                    pe.wait_ge(blocks_moved[u.parity], (u - u.parity).count(MOVED // 2, MOVED))
                else:
                    pe.wait_ge(pT_saved[0], 2 * u.drained(B) + 2)
                    pe.wait_ge(pT_saved[1], 2 * u.drained(B) + 2)
                for c in range(KC):
                    for r in range(R):
                        f = P * c + HD * r
                        last = pe.matmul(bank_o[HD * r:HD * r + HD, c, :], vs[:, u.place, f:f + HD],
                                         prT[u.parity][:, :, KC * r + c, :], start=True, stop=True)
                last.then_inc(oT_ready, 1)

            def output_rows(u):
                product3(bank_a[:], lambda k: o_hi[:, k, :], lambda k: o_lo[:, k, :],
                         lambda k: w_hi[3][:, k, :], lambda k: w_lo[3][:, k, :]).then_inc(rows_ready, 1)

            def step(t, _):
                b = t + 1
                if b.within(B):
                    scores(b, range(KC // 2))
                u = t - 1
                b = t + 3
                if b.within(B):
                    pe.wait_ge(hT_low, b.of_pair.count(1, 2))
                    if (u - 1).within(B):
                        pe.wait_ge(y_done, u.count(1))
                    elif (b - 1).within(B):
                        pe.wait_ge(qk_saved, b.count(2, -1))
                    qk_chunk(b, 0, bank_a)
                if u.within(B):
                    transposed_output(u)
                b = t + 1
                if b.within(B):
                    scores(b, range(KC // 2, KC))
                b = t + 3
                if b.within(B):
                    if (t + LEAD - 1).within(B):
                        pe.wait_ge(hT_low, t.count(1, LEAD))
                    elif (b - 1).within(B):
                        pe.wait_ge(qk_saved, b.count(2))
                    qk_chunk(b, 1, bank_b)
                if u.within(B):
                    if not (u - 1).within(B):
                        pe.wait_ge(w_low, 4)
                    pe.wait_ge(oT_low, u.count(1, 1))
                    pe.wait_ge(qk_saved, (t + 3).count(2, 1))
                    output_rows(u)
                b = t + LEAD
                if b.within(B):
                    if not (b - 1).within(B):
                        pe.wait_ge(ident_set, 2)
                    pe.wait_ge(h_normed, b.count(1, 1))
                    if (t + 3).within(B):
                        pe.wait_ge(qk_saved, (t + 3).count(2, 2))
                    elif (b - 1).within(B):
                        pe.wait_ge(hT_low, b.count(1))
                    for k in range(KC):
                        last = pe.transpose(bank_t[:, k, :], hn[:, b.parity, P * k:P * k + P], ident[:])
                    last.then_inc(hT_ready, 1)
                b = t + 3
                if b.within(B):
                    if (b - 1).within(B):
                        pe.wait_ge(v_saved, b.count(1))
                    else:
                        pe.wait_ge(w_low, 3)
                    hi, lo = h_hi[b.pair_parity], h_lo[b.pair_parity]
                    tok = slice(b.parity * N, b.parity * N + N)
                    product3(bank_c[:], lambda k: hi[:, k, tok], lambda k: lo[:, k, tok],
                             lambda k: w_hi[2][:, k, :], lambda k: w_lo[2][:, k, :]).then_inc(v_ready, 1)

            def transpose_probabilities(t):
                for r in range(R):
                    if r < R - 1:
                        pe.wait_ge(normed, t.count(3, r + 1))
                    else:
                        pe.wait_ge(normed_last, t.count(1, 1))
                    if t.drained(B) == 0 and r == 0:
                        pe.wait_ge(qk_saved, 2 * B)
                    elif t.drained(B) == 0 and r == 1:
                        pe.wait_ge(v_saved, B)
                    else:
                        pe.wait_ge(pT_saved[r % 2], 2 * t.drained(B) + r // 2)
                    for c in range(KC):
                        last = pe.transpose(pT_banks[r % 2][:, c, :], pr[:, KC * r + c, :], ident[:])
                    last.then_inc(pT_ready, 1)

            def drain(t):
                if t.drained(B) == 0:
                    scores(t + 1, range(KC))
                transpose_probabilities(t)
                if t.drained(B) == 0:
                    transposed_output(t - 1)
                    pe.wait_ge(oT_low, t.count(1))
                    pe.wait_ge(y_done, (t - 1).count(1))
                    output_rows(t - 1)
                transposed_output(t)
                if (t + 2).within(B):
                    scores(t + 2, range(KC))
                pe.wait_ge(oT_low, t.count(1, 1))
                pe.wait_ge(y_done, t.count(1))
                output_rows(t)

            steps(pe, step, drain)

        @block.scalar
        def _(act):
            def exponentials(b, groups):
                for r in groups:
                    if r == 0 and not (b - 1).within(B):
                        act.wait_ge(w_low, len(W_NAMES))
                    if r == 0 and (b - 1).within(B):
                        if (b - 1).drained(B) is None:
                            act.wait_ge(blocks_turned, b.count(2))
                        else:
                            act.wait_ge(pT_ready, 4 * (b - 1).drained(B) + 4)
                    if r % 2 == 0:
                        act.wait_ge(max_done, b.count(2, r // 2 + 1))
                    for c in range(KC):
                        i = KC * r + c
                        last = nc.scalar.activation(pr[:, i, :], a[:, i, :], ACT.Exp,
                                                    bias=negmax[:, b.parity, i:i + 1], scale=1.0,
                                                    accum_out=sums[:, b.parity, i:i + 1])
                    last.then_inc(exps, 1)

            def save_qk(b, half, bank):
                c = 2 * b.parity + half
                act.wait_ge(qk_ready, b.count(2, half + 1))
                nc.scalar.copy(qk[:, b.pair_parity, c, :, :].rearrange("p i n -> p (i n)"),
                               bank[:]).then_inc(qk_saved, 1)

            def save_pT(t, r):
                act.wait_ge(pT_ready, 4 * t.drained(B) + r + 1)
                nc.scalar.copy(prT[t.parity][:, :, KC * r:KC * r + KC, :].rearrange("p i c q -> p c i q"),
                               pT_banks[0].rearrange("p c (i q) -> p c i q", i=Q)).then_inc(pT_saved[0], 1)

            def save_v(b):
                act.wait_ge(v_ready, b.count(1, 1))
                nc.scalar.copy(vs[:, b.place, :], bank_c[:]).then_inc(v_saved, 1)

            def high_oT(u):
                act.wait_ge(oT_ready, u.count(1, 1))
                nc.scalar.copy(o_hi[:], bank_o[:]).then_inc(oT_high, 1)

            def normalise_last(b):
                act.wait_ge(inv_live_done, b.count(2, 2))
                for i in range(HEADS - KC, HEADS):
                    last = nc.scalar.mul(pr[:, i, :], pr[:, i, :], inv_live[:, b.parity, i:i + 1])
                last.then_inc(normed_last, 1)

            def high_hT(b):
                act.wait_ge(hT_ready, b.count(1, 1))
                tok = slice(b.parity * N, b.parity * N + N)
                nc.scalar.activation(h_hi[b.pair_parity][:, :, tok], bank_t, ACT.Relu).then_inc(hT_high, 1)

            def high_weight(i):
                act.wait_ge(w_in[i], 16)
                nc.scalar.copy(w_hi[i][:].rearrange("p c n -> p (c n)"), stage[i]).then_inc(w_high, 1)

            def step(t, _):
                if t.within(B):
                    exponentials(t, (3,))
                b = t + 2
                if b.within(B):
                    save_v(b)
                if t.within(B):
                    normalise_last(t)
                b = t + 3
                if b.within(B):
                    save_qk(b, 0, bank_a)
                u = t - 1
                if u.within(B):
                    high_oT(u)
                b = t + 3
                if b.within(B):
                    save_qk(b, 1, bank_b)
                b = t + 1
                if b.within(B):
                    exponentials(b, (0, 1))
                if (t + LEAD).within(B):
                    high_hT(t + LEAD)
                b = t + 1
                if b.within(B):
                    exponentials(b, (2,))

            def drain(t):
                exponentials(t, (3,))
                normalise_last(t)
                if t.drained(B) == 0:
                    save_v(t + 2)
                save_pT(t, 0)
                save_pT(t, 2)
                if t.drained(B) == 0:
                    high_oT(t - 1)
                if (t + 1).within(B):
                    exponentials(t + 1, (0,))
                high_oT(t)
                if (t + 1).within(B):
                    exponentials(t + 1, (1, 2))

            high_hT(Batch(0, 0))
            high_weight(0)
            high_hT(Batch(0, 1))
            high_weight(1)
            high_weight(2)
            steps(act, step, drain, first=2 - LEAD, output_weight=high_weight)

        @block.vector
        def _(dve):
            def low_weight(i):
                dve.wait_ge(w_high, i + 1)
                nc.vector.tensor_tensor(w_lo[i][:].rearrange("p c n -> p (c n)"), stage[i],
                                        w_hi[i][:].rearrange("p c n -> p (c n)").bitcast(F32),
                                        ALU.subtract).then_inc(w_low, 1)

            def statistics(b, halves):
                nc.vector.bn_stats(stats[:, b.parity, :], x_ring(b, halves)).then_inc(stats_done, 1)

            def aggregate(b):
                nc.vector.bn_aggr(moments[:, b.parity, :], stats[:, b.parity, :]).then_inc(moments_done, 1)

            def norm_rows(b, halves):
                dve.wait_ge(rstd_done, b.count(1, 1))
                if (b - 2).within(B):
                    dve.wait_ge(hT_ready, (b - 2).count(1, 1))
                nc.vector.tensor_scalar(hn[:, b.parity, :], x_ring(b, halves), moments[:, b.parity, 0:1],
                                        rstd[:, b.parity, 1:2], ALU.subtract, ALU.mult).then_inc(h_normed, 1)

            def low_hT(b):
                dve.wait_ge(hT_high, b.count(1, 1))
                tok = slice(b.parity * N, b.parity * N + N)
                nc.vector.scalar_tensor_tensor(out=h_lo[b.pair_parity][:, :, tok], in0=bank_t, scalar=0.0,
                                               in1=h_hi[b.pair_parity][:, :, tok].bitcast(F32),
                                               op0=ALU.max, op1=ALU.subtract).then_inc(hT_low, 1)

            def low_oT(u):
                dve.wait_ge(oT_high, u.count(1, 1))
                nc.vector.tensor_tensor(o_lo[:], bank_o[:], o_hi[:].bitcast(F32), ALU.subtract).then_inc(oT_low, 1)

            def residual(u, halves):
                dve.wait_ge(rows_ready, u.count(1, 1))
                if (u - 2).within(B):
                    dve.wait_ge(out_done[u.parity], (u - 2 - u.parity).count(8, 16))
                nc.vector.tensor_tensor(y[:, u.parity, :], bank_a[:], x_ring(u, halves), ALU.add).then_inc(y_done, 1)

            def reciprocals(b, part):
                cols = slice(part * HEADS // 2, (part + 1) * HEADS // 2)
                dve.wait_ge(exps, b.count(4, 2 * part + 2))
                nc.vector.reciprocal(inv[:, cols], sums[:, b.parity, cols]).then_inc(inv_done, 1)

            def live_rows_only(b, part):
                cols = slice(part * HEADS // 2, (part + 1) * HEADS // 2)
                dve.wait_ge(abs_done, b.count(2, part + 1))
                dve.wait_ge(inv_done, b.count(2, part + 1))
                nc.vector.scalar_tensor_tensor(out=inv_live[:, b.parity, cols], in0=absmax[:, b.parity, cols],
                                               scalar=0.0, in1=inv[:, cols], op0=ALU.not_equal,
                                               op1=ALU.mult).then_inc(inv_live_done, 1)

            def turn_blocks(b, part):
                heads = slice(part * HEADS // 2, (part + 1) * HEADS // 2)
                dve.wait_ge(normed, b.count(3, part + 2))
                if part == 1:
                    dve.wait_ge(normed_last, b.count(1, 1))
                if part == 0 and (b - 2).within(B):
                    dve.wait_ge(blocks_moved[b.parity], (b - 2 - b.parity).count(MOVED // 2, MOVED))
                nc.vector.transpose(blocks[b.parity][:, :, heads, :].rearrange("p j h q -> p h j q"),
                                    pr[:, heads, :].rearrange("p h (j m) -> p h j m", j=Q)).then_inc(blocks_turned, 1)

            def biased_max(b, part):
                if part == 0:
                    dve.wait_ge(scores_ready, b.count(1, 1))
                    dve.wait_ge(adj_doubled, b.count(1, 1))
                    if (b - 1).within(B):
                        dve.wait_ge(exps, b.count(4))
                for r in (2 * part, 2 * part + 1):
                    nc.vector.scalar_tensor_tensor(
                        out=a[:, KC * r:KC * r + KC, :], in0=quad[r][:], scalar=SCALE,
                        in1=adj2[:, b.parity:b.parity + 1, :].to_broadcast([P, KC, N]),
                        op0=ALU.mult, op1=ALU.add).then_inc(biased, 1)
                heads = slice(part * HEADS // 2, (part + 1) * HEADS // 2)
                dve.wait_ge(biased, b.count(4, 2 * part + 2))
                nc.vector.tensor_reduce(negmax[:, b.parity, heads], a[:, heads, :], AX.X, ALU.max,
                                        negate=True).then_inc(max_done, 1)

            def row_absmax(b, part):
                heads = slice(part * HEADS // 2, (part + 1) * HEADS // 2)
                nc.vector.tensor_reduce(absmax[:, b.parity, heads], a[:, heads, :], AX.X, ALU.max,
                                        apply_absolute_value=True).then_inc(abs_done, 1)

            def live_first_half(b):
                row_absmax(b, 0)
                reciprocals(b, 0)
                live_rows_only(b, 0)
                row_absmax(b, 1)

            def step(t, halves):
                b = t + LEAD
                if t.within(B):
                    turn_blocks(t, 0)
                if b.within(B):
                    dve.wait_ge(x_in[b.place], b.of_group.count(4, 16))
                if t.within(B):
                    reciprocals(t, 1)
                if t.within(B):
                    live_rows_only(t, 1)
                if b.within(B):
                    statistics(b, halves)
                    dve.wait_ge(stats_done, b.count(1, 1))
                if t.within(B):
                    turn_blocks(t, 1)
                if (t + LEAD).within(B):
                    aggregate(t + LEAD)
                u = t - 1
                if u.within(B):
                    low_oT(u)
                if (t + LEAD).within(B):
                    norm_rows(t + LEAD, halves)
                b = t + 1
                if b.within(B):
                    biased_max(b, 0)
                    biased_max(b, 1)
                    live_first_half(b)
                if u.within(B):
                    residual(u, halves)
                if (t + LEAD).within(B):
                    low_hT(t + LEAD)

            def save_pT(t, r):
                dve.wait_ge(pT_ready, 4 * t.drained(B) + r + 1)
                nc.vector.tensor_copy(prT[t.parity][:, :, KC * r:KC * r + KC, :].rearrange("p i c q -> p c i q"),
                                      pT_banks[1].rearrange("p c (i q) -> p c i q", i=Q)).then_inc(pT_saved[1], 1)

            def drain(t):
                reciprocals(t, 1)
                live_rows_only(t, 1)
                save_pT(t, 1)
                if (t + 1).within(B):
                    biased_max(t + 1, 0)
                save_pT(t, 3)
                if t.drained(B) == 0:
                    low_oT(t - 1)
                if (t + 1).within(B):
                    biased_max(t + 1, 1)
                if t.drained(B) == 0:
                    residual(t - 1, (0, 1))
                low_oT(t)
                if (t + 1).within(B):
                    live_first_half(t + 1)
                residual(t, (0, 1))

            first, second = Batch(0, 0), Batch(0, 1)
            for b in (first, second):
                dve.wait_ge(x_in[b.place], 16)
                statistics(b, (0, 1))
                dve.wait_ge(stats_done, b.count(1, 1))
                aggregate(b)
            norm_rows(first, (0, 1))
            norm_rows(second, (0, 1))
            low_hT(first)
            low_weight(0)
            low_hT(second)
            low_weight(1)
            low_weight(2)
            steps(dve, step, drain, first=2 - LEAD, output_weight=low_weight, uses_x_ring=True)

        @block.gpsimd
        def _(pool):
            nc.gpsimd.memset(ident[:], 0.0).then_inc(ident_set, 1)
            pool.wait_ge(ident_set, 1)
            nc.gpsimd.affine_select(out=ident[:], in_=ident[:], compare_op=ALU.not_equal, fill=1.0, base=0,
                                    pattern=[[-1, P]], channel_multiplier=1).then_inc(ident_set, 1)
            nc.gpsimd.memset(consts[:, 0:1], EPS).then_inc(const_set, 1)
            nc.gpsimd.memset(consts[:, 1:2], -0.5).then_inc(const_set, 1)
            pool.wait_ge(const_set, 2)

            def double_adj(b):
                pool.wait_ge(adj_in[b.place], b.of_group.count(4, 16))
                if (b - 2).within(B):
                    pool.wait_ge(biased, (b - 2).count(4, 4))
                nc.gpsimd.tensor_tensor(adj2[:, b.parity, :], adjs[:, b.place, :], adjs[:, b.place, :],
                                        ALU.add).then_inc(adj_doubled, 1)

            def normalise(b, groups):
                for r in groups:
                    if r % 2 == 0:
                        pool.wait_ge(inv_live_done, b.count(2, r // 2 + 1))
                    heads = slice(KC * r, KC * r + KC)
                    nc.gpsimd.tensor_tensor(pr[:, heads, :], pr[:, heads, :],
                                            inv_live[:, b.parity, heads].unsqueeze(2).to_broadcast([P, KC, N]),
                                            ALU.mult).then_inc(normed, 1)

            def step(t, _):
                if t.within(B):
                    normalise(t, (2,))
                b = t + LEAD
                if b.within(B):
                    pool.wait_ge(moments_done, b.count(1, 1))
                    nc.gpsimd.tensor_tensor(rstd[:, b.parity, 0:1], moments[:, b.parity, 1:2], consts[:, 0:1],
                                            ALU.add).then_inc(var_eps, 1)
                    pool.wait_ge(var_eps, b.count(1, 1))
                    nc.gpsimd.tensor_tensor(rstd[:, b.parity, 1:2], rstd[:, b.parity, 0:1], consts[:, 1:2],
                                            ALU.pow).then_inc(rstd_done, 1)
                b = t + 2
                if b.within(B):
                    double_adj(b)
                b = t + 1
                if b.within(B):
                    normalise(b, (0, 1))

            steps(pool, step, lambda t: step(t, None))


_INS = ["x", "adj", "L0_gnn_Wq", "L0_gnn_Wk", "L0_gnn_Wv", "L0_gnn_Wo"]


def kernel(**inputs):
    import numpy as np
    import concourse.bacc as bacc
    from concourse.bass_utils import run_bass_kernel_spmd

    nc = bacc.Bacc("TRN2", target_bir_lowering=False, num_devices=1)
    arrays, args = {}, []
    for name in _INS:
        a = np.asarray(inputs[name])
        a = np.ascontiguousarray(a.T if a.ndim == 2 else a)
        arrays[f"in_{name}"] = a
        args.append(nc.dram_tensor(f"in_{name}", a.shape, mybir.dt.from_np(a.dtype), kind="ExternalInput").ap())
    shape = inputs["x"].shape
    args.append(nc.dram_tensor("out_0", shape, F32, kind="ExternalOutput").ap())
    preln_graph_attention(nc, *args)
    r = run_bass_kernel_spmd(nc, [arrays], core_ids=[0])
    return r.results[0]["out_0"]
```
